# Optimizing a Trainium2 kernel written in Bass

```python
import numpy as np
import jax
import jax.numpy as jnp

def _softmax(x, axis=-1):
    return jax.nn.softmax(x, axis=axis)

def _gelu(x):
    return jax.nn.gelu(x, approximate=True)

def _silu(x):
    return jax.nn.silu(x)

def _sigmoid(x):
    return jax.nn.sigmoid(x)

def _layernorm(x, axis=-1, eps=1e-05):
    m = jnp.mean(x, axis=axis, keepdims=True)
    v = jnp.var(x, axis=axis, keepdims=True)
    return (x - m) / jnp.sqrt(v + eps)

def _scatter_add(tgt, idx, src, axis=0):
    return tgt.at[idx].add(src)

def _segment_sum(src, seg, n):
    return jax.ops.segment_sum(src, seg, n)
kernel_name = 'mk_conv_seq_d2_conv_nchw192_r2_a106ce'

def setup_inputs(seed: int=0):
    np.random.seed(seed)
    _w = jnp.asarray

    def _rec_inputs():
        import jax
        import jax.numpy as jnp
        _gk = jax.random.key(seed)
        x = -4.65e-05 + 0.9999 * jax.random.normal(jax.random.fold_in(_gk, 1), (4, 96, 128, 128), jnp.float32)
        return x
    x = _rec_inputs()

    def _L0_conv_setup():
        import jax, jax.numpy as jnp
        import numpy as np
        DIM = 96
        K = 3
        RED = 4
        B, H, W = (4, 128, 128)
        EPS = 1e-05

        def _make_mask():
            m = np.ones((DIM, 1, K, K), np.float32)
            m[:, :, K // 2, K // 2:] = 0.0
            m[:, :, K // 2 + 1:] = 0.0
            return jnp.asarray(m)
        MASK = _make_mask()
        key = jax.random.key(seed)
        ks = jax.random.split(key, 4)
        r = DIM // RED
        return {'x': jax.random.normal(ks[0], (B, DIM, H, W), jnp.float32), 'w1': jax.random.normal(ks[1], (r, DIM), jnp.float32) * 0.05, 'gamma': jnp.ones((r,), jnp.float32), 'beta': jnp.zeros((r,), jnp.float32), 'running_mean': jnp.zeros((r,), jnp.float32), 'running_var': jnp.ones((r,), jnp.float32), 'w2': jax.random.normal(ks[2], (DIM * K * K, r), jnp.float32) * 0.05, 'b2': jnp.zeros((DIM * K * K,), jnp.float32), 'bias': jnp.zeros((DIM,), jnp.float32)}
    _L0_conv_all = _L0_conv_setup()
    _L0_conv_in = {k: v for k, v in _L0_conv_all.items() if k in ('w1', 'gamma', 'beta', 'running_mean', 'running_var', 'w2', 'b2', 'bias')}
    del _L0_conv_all

    def _L1_conv_setup():
        import jax, jax.numpy as jnp
        import numpy as np
        REPARAM_OFFSET = 2.0 ** (-18)
        PEDESTAL = REPARAM_OFFSET ** 2
        BETA_MIN = 1e-06
        BOUND_BETA = (BETA_MIN + PEDESTAL) ** 0.5
        BOUND_GAMMA = PEDESTAL ** 0.5
        INVERSE = False

        def _nn_init(v):
            return jnp.sqrt(jnp.maximum(v + PEDESTAL, PEDESTAL))

        def _nn_reparam(v, bound):
            return jnp.square(jnp.maximum(v, bound)) - PEDESTAL
        key = jax.random.key(seed)
        N, C, H, W = (4, 96, 128, 128)
        x = jax.random.normal(key, (N, C, H, W), dtype=jnp.float32)
        beta = _nn_init(jnp.ones((C,), dtype=jnp.float32))
        gamma = _nn_init(0.1 * jnp.eye(C, dtype=jnp.float32))
        return {'x': x, 'beta': beta, 'gamma': gamma}
    _L1_conv_all = _L1_conv_setup()
    _L1_conv_in = {k: v for k, v in _L1_conv_all.items() if k in ('beta', 'gamma')}
    del _L1_conv_all
    return {'x': x, 'L0_conv_w1': _L0_conv_in['w1'], 'L0_conv_gamma': _L0_conv_in['gamma'], 'L0_conv_beta': _L0_conv_in['beta'], 'L0_conv_running_mean': _L0_conv_in['running_mean'], 'L0_conv_running_var': _L0_conv_in['running_var'], 'L0_conv_w2': _L0_conv_in['w2'], 'L0_conv_b2': _L0_conv_in['b2'], 'L0_conv_bias': _L0_conv_in['bias'], 'L1_conv_beta': _L1_conv_in['beta'], 'L1_conv_gamma': _L1_conv_in['gamma']}

def reference(x, L0_conv_w1, L0_conv_gamma, L0_conv_beta, L0_conv_running_mean, L0_conv_running_var, L0_conv_w2, L0_conv_b2, L0_conv_bias, L1_conv_beta, L1_conv_gamma):
    import jax
    import jax.numpy as jnp

    def _L0_conv_ref(x, w1, gamma, beta, running_mean, running_var, w2, b2, bias):
        import jax, jax.numpy as jnp
        import numpy as np
        DIM = 96
        K = 3
        RED = 4
        B, H, W = (4, 128, 128)
        EPS = 1e-05

        def _make_mask():
            m = np.ones((DIM, 1, K, K), np.float32)
            m[:, :, K // 2, K // 2:] = 0.0
            m[:, :, K // 2 + 1:] = 0.0
            return jnp.asarray(m)
        MASK = _make_mask()
        b, c, h, w = x.shape
        pooled = x.mean(axis=(2, 3))
        t = pooled @ w1.T
        t = gamma * (t - running_mean) * jax.lax.rsqrt(running_var + EPS) + beta
        t = jax.nn.relu(t)
        wt = t @ w2.T + b2
        wt = wt.reshape(b * DIM, 1, K, K) * jnp.tile(MASK, (b, 1, 1, 1))
        out = jax.lax.conv_general_dilated(x.reshape(1, b * c, h, w), wt, window_strides=(1, 1), padding=((1, 1), (1, 1)), feature_group_count=b * DIM, dimension_numbers=('NCHW', 'OIHW', 'NCHW'))
        out = out + jnp.tile(bias, (b,))[None, :, None, None]
        return out.reshape(b, c, h, w)

    def _L1_conv_ref(x, beta, gamma):
        import jax, jax.numpy as jnp
        import numpy as np
        REPARAM_OFFSET = 2.0 ** (-18)
        PEDESTAL = REPARAM_OFFSET ** 2
        BETA_MIN = 1e-06
        BOUND_BETA = (BETA_MIN + PEDESTAL) ** 0.5
        BOUND_GAMMA = PEDESTAL ** 0.5
        INVERSE = False

        def _nn_init(v):
            return jnp.sqrt(jnp.maximum(v + PEDESTAL, PEDESTAL))

        def _nn_reparam(v, bound):
            return jnp.square(jnp.maximum(v, bound)) - PEDESTAL
        beta_eff = _nn_reparam(beta, BOUND_BETA)
        gamma_eff = _nn_reparam(gamma, BOUND_GAMMA)
        x2 = x * x
        denom_sq = jnp.einsum('nchw,ic->nihw', x2, gamma_eff)
        denom_sq = denom_sq + beta_eff[None, :, None, None]
        norm = jnp.sqrt(denom_sq) if INVERSE else jax.lax.rsqrt(denom_sq)
        return x * norm

    def _gn(v, G=32, eps=1e-05):
        B_, C_, H_, W_ = v.shape
        g = v.reshape(B_, G, C_ // G, H_, W_)
        m = jnp.mean(g, axis=(2, 3, 4), keepdims=True)
        s = jnp.var(g, axis=(2, 3, 4), keepdims=True)
        return ((g - m) / jnp.sqrt(s + eps)).reshape(v.shape)

    def _ln_c(v, eps=1e-06):
        m = jnp.mean(v, axis=1, keepdims=True)
        s = jnp.var(v, axis=1, keepdims=True)
        return (v - m) / jnp.sqrt(s + eps)

    def _ln_t(v, eps=1e-05):
        m = jnp.mean(v, axis=-1, keepdims=True)
        s = jnp.var(v, axis=-1, keepdims=True)
        return (v - m) / jnp.sqrt(s + eps)

    def _to_tokens(v):
        B_, C_, H_, W_ = v.shape
        return v.reshape(B_, C_, H_ * W_).transpose(0, 2, 1)

    def _from_tokens(t, like):
        B_, C_, H_, W_ = like.shape
        return t.transpose(0, 2, 1).reshape(B_, C_, H_, W_)
    x = _L0_conv_ref(x, L0_conv_w1, L0_conv_gamma, L0_conv_beta, L0_conv_running_mean, L0_conv_running_var, L0_conv_w2, L0_conv_b2, L0_conv_bias)
    x = _L1_conv_ref(x, L1_conv_beta, L1_conv_gamma)
    return x

_drawn_inputs = setup_inputs


def setup_inputs(seed=0):
    import zlib

    import numpy as np

    out = dict(_drawn_inputs(seed))
    spreads = {'L0_conv_gamma': (1.0, 0.6),
     'L0_conv_beta': (0.0, 0.1),
     'L0_conv_running_mean': (0.0, 0.1),
     'L0_conv_running_var': (1.0, 0.6),
     'L0_conv_b2': (0.0, 0.1),
     'L0_conv_bias': (0.0, 0.1),
     'L1_conv_beta': (1.0, 0.2)}
    factors = {'L0_conv_w1': 8.0, 'L1_conv_gamma': 5.155}
    for name, (base, spread) in spreads.items():
        noise = np.random.default_rng([zlib.crc32(name.encode()), seed]).standard_normal(out[name].shape)
        drawn = base * np.exp(spread * noise) if base else spread * noise
        out[name] = jnp.asarray(drawn.astype(out[name].dtype))
    for name, factor in factors.items():
        out[name] = (out[name] * factor).astype(out[name].dtype)
    return out
```

```python
from contextlib import ExitStack

import numpy as np

import concourse.bass as bass
from concourse import mybir

F32 = mybir.dt.float32
BF16 = mybir.dt.bfloat16
ALU = mybir.AluOpType
ACT = mybir.ActivationFunctionType
AX = mybir.AxisListType

BN_EPS = 1e-5
OFFSET = 2.0 ** -18
PEDESTAL = OFFSET ** 2
BETA_BOUND = (1e-6 + PEDESTAL) ** 0.5
GAMMA_BOUND = PEDESTAL ** 0.5

SLOTS = 3
QUARTERS = 4
UP_LEFT, UP, UP_RIGHT, LEFT = range(4)
TAPS = 4
TAP_AT = {UP_LEFT: (0, 0), UP: (0, 1), UP_RIGHT: (0, 2), LEFT: (1, 0)}


def conv_gdn(nc, x, w1t, bn, w2t, b2, bias, beta, gammat, out):
    B, C, H, W = x.shape
    R = w1t.shape[1]
    K2 = w2t.shape[1] // C
    QR = H // QUARTERS
    CD = C // SLOTS
    P = C + CD
    ROWS, COLS = QR + 1, W + 1
    UR = 8
    UNITS = QR // UR
    N = UR * W
    BANK = 512
    CUT = QR // 2
    PIECES = [(h, s) for h in range(2) for s in range(SLOTS)]
    CONVS = UNITS * SLOTS
    NORMS = UNITS * QUARTERS
    assert P == 128 and N % BANK == 0 and UNITS % 2 == 0

    ctx = ExitStack()
    with ctx:
        def sb(name, shape, dt=F32):
            return ctx.enter_context(nc.sbuf_tensor(name, shape, dt))

        def sem(name):
            return ctx.enter_context(nc.semaphore(name))

        ximg = sb("ximg", [P, 2, SLOTS, ROWS * COLS])
        y = sb("y", [P, 2, SLOTS, N])
        yd = sb("yd", [C, 2, N])
        sq = sb("sq", [C, QUARTERS, N])
        norm = sb("norm", [C, QUARTERS, N])
        pool_out = sb("pool_out", [P, 2, (QR - CUT + 1) * COLS], BF16)
        part = sb("part", [P, len(PIECES)])
        taps = sb("taps", [P, 2 * SLOTS * TAPS])
        w1s = sb("w1s", [P, SLOTS, R])
        w2s = sb("w2s", [R + 1, C * K2])
        w2p = sb("w2p", [R + 1, TAPS, SLOTS, P])
        hid = sb("hid", [R + 1, 1])
        bnp = sb("bnp", [R, 4])
        bnw = sb("bnw", [R, 8])
        bias_s = sb("bias_s", [P, SLOTS])
        beta_s = sb("beta_s", [C, 1])
        beta_e = sb("beta_e", [C, 1])
        gam_s = sb("gam_s", [C, C])
        gam_e = sb("gam_e", [C, C])
        warm = sb("warm", [P, 1])

        acc = ctx.enter_context(nc.psum_tensor("acc", [P, 2, N], F32))
        den = ctx.enter_context(nc.psum_tensor("den", [P, 2, N], F32))
        hid_ps = den[0:R, 1, 0:1]
        taps_ps = den[0:P, 1, BANK:BANK + SLOTS * TAPS]

        par_loaded = sem("par_loaded")
        x_loaded = [sem(f"x_loaded{i}") for i in range(len(PIECES))]
        pads_zeroed = sem("pads_zeroed")
        ones_set = sem("ones_set")
        setup = sem("setup")
        setup_own = sem("setup_own")
        bn_root = sem("bn_root")
        consts_ready = sem("consts_ready")
        pooled_act = sem("pooled_act")
        pooled_dve = sem("pooled_dve")
        hid_summed = sem("hid_summed")
        hid_ready = sem("hid_ready")
        taps_summed = sem("taps_summed")
        taps_ready = sem("taps_ready")
        based = sem("based")
        tap_added = sem("tap_added")
        convolved = sem("convolved")
        d_moved = [sem(f"d_moved{i}") for i in range(2)]
        squared = sem("squared")
        summed = sem("summed")
        normed = sem("normed")
        warmed = sem("warmed")
        scaled = sem("scaled")
        stored = [sem(f"stored{g}") for g in range(QUARTERS)]

        def conv_no(b, u, s):
            return b * CONVS + (u * SLOTS + s)

        def norm_no(b, u, g):
            return b * NORMS + (u * QUARTERS + g)

        def unit_no(b, u):
            return b * UNITS + u

        def above_zero(n):
            return not isinstance(n, int) or n > 0

        def img(b):
            if isinstance(b, int):
                return ximg[:, b % 2]
            return ximg[:, bass.ds(b % 2, 1)].rearrange("p o s n -> p (o s) n")

        def img_rows(b, s):
            return img(b)[:, s, :].rearrange("p (r c) -> p r c", c=COLS)

        def tap_in(b, u, s, tap):
            r, c = TAP_AT[tap]
            at = (r + u * UR) * COLS + c
            return img(b)[:, s, at:at + UR * COLS].rearrange("p (r c) -> p r c", c=COLS)[:, :, 0:W]

        def tap_w(b, s, tap):
            at = s * TAPS + tap
            if isinstance(b, int):
                at += (b % 2) * SLOTS * TAPS
                return taps[:, at:at + 1]
            return taps[:, bass.ds((b % 2) * (SLOTS * TAPS) + at, 1)]

        def piece_rows(h):
            return (0, CUT) if h == 0 else (CUT, ROWS)

        def in_rows(ap):
            return ap.rearrange("p (r c) -> p r c", c=W)

        def quarter(u, g):
            return y[0:C, u % 2, g] if g < SLOTS else yd[:, u % 2]

        def out_rows(b, u, g):
            r = g * QR + u * UR
            if isinstance(b, int):
                return out[b, :, r:r + UR, :].rearrange("c r w -> c (r w)")
            return out[bass.ds(b, 1), :, r:r + UR, :].rearrange("o c r w -> (o c) (r w)")

        def load_piece(sp, b, i):
            h, s = PIECES[i]
            r0, r1 = piece_rows(h)
            src = x[b] if isinstance(b, int) else x[bass.ds(b, 1)].rearrange("o c h w -> (o c) h w")
            top = max(r0, 1) if s == 0 else r0
            a = s * QR - 1
            sp.dma_start(img_rows(b, s)[0:C, top:r1, 1:COLS], src[:, a + top:a + r1, :]).then_inc(x_loaded[i], 16)
            a = SLOTS * QR - 1
            sp.dma_start(img_rows(b, s)[C:P, r0:r1, 1:COLS],
                         src[s * CD:(s + 1) * CD, a + r0:a + r1, :]).then_inc(x_loaded[i], 16)

        def move_d(sp, b, u):
            for s in range(SLOTS):
                sp.wait_ge(convolved, conv_no(b, u, s) + 1)
                sp.dma_start(yd[s * CD:(s + 1) * CD, u % 2], y[C:P, u % 2, s]).then_inc(d_moved[u % 2], 16)

        def store(sp, b, u, g):
            sp.wait_ge(scaled, norm_no(b, u, g) + 1)
            sp.dma_start(out_rows(b, u, g), norm[:, g]).then_inc(stored[g], 16)

        def load_next(sp, b, h):
            for i, (hh, s) in enumerate(PIECES):
                if hh == h:
                    sp.wait_ge(convolved, conv_no(b, 2 * h + 1, s) + 1)
                    sp.wait_ge(x_loaded[i], 32 * (b + 2))
                    load_piece(sp, b + 2, i)

        def sp_image(sp, b, last, loads):
            for u in range(UNITS):
                if u < UNITS - 1:
                    move_d(sp, b, u + 1)
                elif not last:
                    move_d(sp, b + 1, 0)
                if loads and u == 1:
                    load_next(sp, b, 0)
                for g in range(QUARTERS):
                    store(sp, b, u, g)
                if loads and u == UNITS - 1:
                    load_next(sp, b, 1)

        def pool_on_act(act, b, i, k):
            h, s = PIECES[i]
            r0, r1 = piece_rows(h)
            r0 = max(r0, 1)
            act.wait_ge(x_loaded[i], 32 * (b + 1))
            src = img(b)[:, s, r0 * COLS:r1 * COLS]
            n = k if isinstance(b, int) and b == 0 else (b - 1) * len(PIECES) + ACT_POOLS + k
            if above_zero(n - 1):
                act.wait_ge(pooled_act, n - 1)
            nc.scalar.activation(pool_out[:, k % 2, 0:(r1 - r0) * COLS], src, ACT.Copy,
                                 accum_out=part[:, i:i + 1]).then_inc(pooled_act, 1)

        def hidden(act, b):
            act.wait_ge(hid_summed, b + 1)
            nc.scalar.activation(hid[0:R, :], hid_ps, ACT.Relu, bias=bnw[:, 1:2], scale=bnw[:, 0:1]).then_inc(hid_ready, 1)

        def base(act, b, u, s):
            n = conv_no(b, u, s)
            if above_zero(n - 1):
                act.wait_ge(convolved, n - 1)
            if u == 0 and s == 0:
                act.wait_ge(taps_ready, b + 1)
            nc.scalar.activation(in_rows(acc[:, n_parity(u, s)]), tap_in(b, u, s, UP), ACT.Identity,
                                 bias=bias_s[:, s:s + 1], scale=tap_w(b, s, UP)).then_inc(based, 1)

        def n_parity(u, s):
            return (u * SLOTS + s) % 2

        def square(act, b, u, g):
            if g == 0 and above_zero(norm_no(b, u, 0)):
                act.wait_ge(summed, norm_no(b, u, 0))
            if g < SLOTS:
                act.wait_ge(convolved, conv_no(b, u, g) + 1)
            else:
                act.wait_ge(d_moved[u % 2], d_count(b, u))
            nc.scalar.activation(sq[:, g], quarter(u, g), ACT.Square).then_inc(squared, 1)

        def d_count(b, u):
            return (b * (UNITS // 2) + (u // 2 + 1)) * (16 * SLOTS)

        def rsqrt(act, b, u, g):
            act.wait_ge(summed, norm_no(b, u, g) + 1)
            if above_zero(unit_no(b, u)):
                act.wait_ge(stored[g], unit_no(b, u) * 16)
            nc.scalar.activation(norm[:, g], den[0:C, g % 2], ACT.Abs_reciprocal_sqrt,
                                 bias=beta_e[:, 0:1]).then_inc(normed, 1)

        def act_unit(act, b, u, last):
            nb, nu = (b, u + 1) if u < UNITS - 1 else (b + 1, 0)
            conv = not (last and u == UNITS - 1)
            pool = not last and u < UNITS - 1
            square(act, b, u, 0)
            if pool:
                pool_on_act(act, b + 1, 2 * u, 2 * u)
            if conv:
                base(act, nb, nu, 1)
            square(act, b, u, 1)
            rsqrt(act, b, u, 0)
            square(act, b, u, 2)
            if pool:
                pool_on_act(act, b + 1, 2 * u + 1, 2 * u + 1)
            if conv:
                base(act, nb, nu, 2)
            rsqrt(act, b, u, 1)
            square(act, b, u, 3)
            rsqrt(act, b, u, 2)
            if not last and u == TAPS_UNIT:
                hidden(act, b + 1)
            rsqrt(act, b, u, 3)
            if not (last and u >= UNITS - 2):
                fb, fu = (nb, nu + 1) if nu < UNITS - 1 else (nb + 1, 0)
                base(act, fb, fu, 0)

        def tap_sums(pe, b):
            if isinstance(b, int) and b == 0:
                pe.wait_ge(pooled_dve, DVE_POOLS)
                pe.wait_ge(pooled_act, ACT_POOLS)
            else:
                pe.wait_ge(pooled_act, ACT_POOLS + b * len(PIECES))
                pe.wait_ge(normed, norm_no(b - 1, TAPS_UNIT, 1) + 1)
            for i, (h, s) in enumerate(PIECES):
                last = nc.tensor.matmul(hid_ps, w1s[:, s, :], part[:, i:i + 1], start=i == 0, stop=i == len(PIECES) - 1)
            last.then_inc(hid_summed, 1)
            pe.wait_ge(hid_ready, b + 1)
            for s in range(SLOTS):
                for t in range(TAPS):
                    at = BANK + s * TAPS + t
                    last = nc.tensor.matmul(den[:, 1, at:at + 1], w2p[:, t, s, :], hid[:, :], start=True, stop=True)
            last.then_inc(taps_summed, 1)

        def denominators(pe, b, u, g, last=False):
            n = norm_no(b, u, g)
            pe.wait_ge(squared, n + 1)
            if above_zero(n - 1):
                pe.wait_ge(normed, n - 1)
            if not last and (u, g) in ((0, 1), (TAPS_UNIT, 3)):
                pe.wait_ge(taps_ready, b + 1 if u == 0 else b + 2)
            for j in range(0, N, BANK):
                ins = nc.tensor.matmul(den[0:C, g % 2, j:j + BANK], gam_e[:, :], sq[:, g, j:j + BANK], start=True, stop=True)
            ins.then_inc(summed, 1)

        def pe_image(pe, b):
            for u in range(UNITS):
                for g in range(QUARTERS):
                    if (u, g) == (TAPS_UNIT, 3):
                        tap_sums(pe, b + 1)
                    denominators(pe, b, u, g)

        def read_taps(dve, b):
            dve.wait_ge(taps_summed, b + 1)
            if isinstance(b, int):
                dst = taps[:, (b % 2) * SLOTS * TAPS:(b % 2 + 1) * SLOTS * TAPS]
            else:
                dst = taps[:, bass.ds((b % 2) * (SLOTS * TAPS), SLOTS * TAPS)]
            nc.vector.tensor_copy(dst, taps_ps).then_inc(taps_ready, 1)

        def conv(dve, b, u, s):
            n = conv_no(b, u, s)
            a = in_rows(acc[:, n_parity(u, s)])
            dve.wait_ge(based, n + 1)
            for k, tap in enumerate((UP_LEFT, UP_RIGHT)):
                nc.vector.scalar_tensor_tensor(out=a, in0=tap_in(b, u, s, tap), scalar=tap_w(b, s, tap), in1=a,
                                               op0=ALU.mult, op1=ALU.add).then_inc(tap_added, 1)
                dve.wait_ge(tap_added, 2 * n + (k + 1))
            if above_zero(norm_no(b, u, 0) - QUARTERS):
                dve.wait_ge(scaled, norm_no(b, u, 0) - QUARTERS)
            nc.vector.scalar_tensor_tensor(out=in_rows(y[:, u % 2, s]), in0=tap_in(b, u, s, LEFT), scalar=tap_w(b, s, LEFT),
                                           in1=a, op0=ALU.mult, op1=ALU.add).then_inc(convolved, 1)

        def dve_image(dve, b):
            for u in range(1, UNITS):
                for s in range(SLOTS):
                    conv(dve, b, u, s)
                    if u == TAPS_UNIT + 1 and s == 1:
                        read_taps(dve, b + 1)
            for s in range(SLOTS):
                conv(dve, b + 1, 0, s)

        def scale(pool, b, u, g):
            pool.wait_ge(normed, norm_no(b, u, g) + 1)
            if g == SLOTS:
                pool.wait_ge(d_moved[u % 2], d_count(b, u))
            nc.gpsimd.tensor_tensor(norm[:, g], quarter(u, g), norm[:, g], ALU.mult).then_inc(scaled, 1)

        ACT_POOLS = 4
        DVE_POOLS = len(PIECES) - ACT_POOLS
        TAPS_UNIT = UNITS - 2
        ACT_ORDER = (0, 2, 4, 5)
        DVE_ORDER = (1, 3)
        N_PAR = 2 + 4 * SLOTS + 4 + 2
        block = ctx.enter_context(nc.Block())

        @block.sync
        def _(sp):
            sp.wait_ge(pads_zeroed, 1)
            for i in range(len(PIECES)):
                load_piece(sp, 0, i)
            for i in range(len(PIECES)):
                sp.wait_ge(x_loaded[i], 32)
                load_piece(sp, 1, i)
            move_d(sp, 0, 0)
            for b in range(B - 2):
                sp_image(sp, b, False, True)
            sp_image(sp, B - 2, False, False)
            sp_image(sp, B - 1, True, False)
            for g in range(QUARTERS):
                sp.wait_ge(stored[g], 16 * UNITS * B)

        @block.scalar
        def _(act):
            act.dma_start(w2s[0:R, :], w2t[:, :]).then_inc(par_loaded, 16)
            act.dma_start(w2s[R:R + 1, :], b2[:, :]).then_inc(par_loaded, 16)
            for s in range(SLOTS):
                act.dma_start(w1s[0:C, s, :], w1t[:, :]).then_inc(par_loaded, 16)
                act.dma_start(w1s[C:P, s, :], w1t[s * CD:(s + 1) * CD, :]).then_inc(par_loaded, 16)
                act.dma_start(bias_s[0:C, s:s + 1], bias[:, :]).then_inc(par_loaded, 16)
                act.dma_start(bias_s[C:P, s:s + 1], bias[s * CD:(s + 1) * CD, :]).then_inc(par_loaded, 16)
            for i in range(4):
                act.dma_start(bnp[:, i:i + 1], bn[i]).then_inc(par_loaded, 16)
            act.dma_start(beta_s[:, :], beta[:, :]).then_inc(par_loaded, 16)
            act.dma_start(gam_s[:, :], gammat[:, :]).then_inc(par_loaded, 16)
            act.wait_ge(ones_set, 1)
            nc.scalar.activation(warm[:, :], warm[:, :], ACT.Abs_reciprocal_sqrt).then_inc(warmed, 1)
            act.wait_ge(setup, 1)
            nc.scalar.activation(bnw[:, 3:4], bnw[:, 2:3], ACT.Abs_reciprocal_sqrt).then_inc(bn_root, 1)
            for i in range(0, ACT_POOLS):
                pool_on_act(act, 0, ACT_ORDER[i], i)
            act.wait_ge(consts_ready, 1)
            hidden(act, 0)
            base(act, 0, 0, 0)
            base(act, 0, 0, 1)
            base(act, 0, 0, 2)
            base(act, 0, 1, 0)
            for u in range(UNITS):
                act_unit(act, 0, u, False)
            with act.Fori(1, B - 1) as b:
                for u in range(UNITS):
                    act_unit(act, b, u, False)
            for u in range(UNITS):
                act_unit(act, B - 1, u, True)

        @block.tensor
        def _(pe):
            pe.wait_ge(consts_ready, 1)
            tap_sums(pe, 0)
            pe_image(pe, 0)
            with pe.Fori(1, B - 1) as b:
                pe_image(pe, b)
            for u in range(UNITS):
                for g in range(QUARTERS):
                    denominators(pe, B - 1, u, g, last=True)

        @block.vector
        def _(dve):
            nc.vector.memset(warm[:, :], 1.0).then_inc(ones_set, 1)
            nc.vector.memset(hid[:, :], 1.0).then_inc(setup_own, 1)
            dve.wait_ge(par_loaded, 16 * N_PAR)
            nc.vector.tensor_scalar(bnw[:, 2:3], bnp[:, 3:4], BN_EPS, None, ALU.add).then_inc(setup, 1)
            step = [1]

            def chained(ins):
                step[0] += 1
                ins.then_inc(setup_own, 1)
                dve.wait_ge(setup_own, step[0])

            chained(nc.vector.tensor_scalar(gam_s[:, :], gam_s[:, :], GAMMA_BOUND, None, ALU.max))
            chained(nc.vector.tensor_tensor(gam_e[:, :], gam_s[:, :], gam_s[:, :], ALU.mult))
            chained(nc.vector.tensor_scalar(gam_e[:, :], gam_e[:, :], PEDESTAL, None, ALU.subtract))
            chained(nc.vector.tensor_scalar(beta_s[:, :], beta_s[:, :], BETA_BOUND, None, ALU.max))
            chained(nc.vector.tensor_tensor(beta_e[:, :], beta_s[:, :], beta_s[:, :], ALU.mult))
            chained(nc.vector.tensor_scalar(beta_e[:, :], beta_e[:, :], PEDESTAL, None, ALU.subtract))
            by_tap = w2s[:, :].rearrange("r (c k) -> r k c", k=K2)
            for t in range(TAPS):
                for s in range(SLOTS):
                    nc.vector.tensor_copy(w2p[:, t, s, 0:C], by_tap[:, t, :]).then_inc(setup_own, 1)
                    nc.vector.tensor_copy(w2p[:, t, s, C:P], by_tap[:, t, s * CD:(s + 1) * CD]).then_inc(setup_own, 1)
                    step[0] += 2
            dve.wait_ge(bn_root, 1)
            v, r, q = bnw[:, 2:3], bnw[:, 3:4], bnw[:, 4:5]
            for _ in range(2):
                chained(nc.vector.tensor_tensor(q, r, r, ALU.mult))
                chained(nc.vector.tensor_tensor(q, q, v, ALU.mult))
                chained(nc.vector.tensor_scalar(q, q, -0.5, 1.5, ALU.mult, ALU.add))
                chained(nc.vector.tensor_tensor(r, r, q, ALU.mult))
            chained(nc.vector.tensor_tensor(r, r, bnp[:, 0:1], ALU.mult))
            chained(nc.vector.tensor_tensor(q, r, bnp[:, 2:3], ALU.mult))
            chained(nc.vector.tensor_tensor(bnw[:, 1:2], bnp[:, 1:2], q, ALU.subtract))
            nc.vector.tensor_scalar(bnw[:, 0:1], r, 1.0 / (H * W), None, ALU.mult).then_inc(consts_ready, 1)
            for i in range(DVE_POOLS):
                j = DVE_ORDER[i]
                h, s = PIECES[j]
                r0, r1 = piece_rows(h)
                r0 = max(r0, 1)
                dve.wait_ge(x_loaded[j], 32)
                nc.vector.reduce_sum(part[:, j:j + 1], img(0)[:, s, r0 * COLS:r1 * COLS],
                                     AX.X).then_inc(pooled_dve, 1)
            read_taps(dve, 0)
            dve.wait_ge(taps_ready, 1)
            for s in range(SLOTS):
                conv(dve, 0, 0, s)
            dve_image(dve, 0)
            with dve.Fori(1, B - 1) as b:
                dve_image(dve, b)
            for u in range(1, UNITS):
                for s in range(SLOTS):
                    conv(dve, B - 1, u, s)

        @block.gpsimd
        def _(pool):
            nc.gpsimd.memset(ximg[:, :, :, :].rearrange("p b s (r c) -> p (b s r) c", c=COLS)[:, :, 0:1], 0.0)
            nc.gpsimd.memset(ximg[0:C, :, 0, 1:COLS], 0.0).then_inc(pads_zeroed, 1)
            with pool.Fori(0, B) as b:
                for u in range(UNITS):
                    for g in range(QUARTERS):
                        scale(pool, b, u, g)


_OUT = (4, 96, 128, 128)


def kernel(x, L0_conv_w1, L0_conv_gamma, L0_conv_beta, L0_conv_running_mean, L0_conv_running_var, L0_conv_w2,
           L0_conv_b2, L0_conv_bias, L1_conv_beta, L1_conv_gamma):
    import concourse.bacc as bacc
    from concourse.bass_utils import run_bass_kernel_spmd

    def column(a):
        return np.ascontiguousarray(np.asarray(a).reshape(-1, 1))

    arrays = {
        "x": np.ascontiguousarray(x),
        "w1t": np.ascontiguousarray(np.asarray(L0_conv_w1).T),
        "bn": np.stack([column(a) for a in (L0_conv_gamma, L0_conv_beta, L0_conv_running_mean, L0_conv_running_var)]),
        "w2t": np.ascontiguousarray(np.asarray(L0_conv_w2).T),
        "b2": np.ascontiguousarray(np.asarray(L0_conv_b2).reshape(1, -1)),
        "bias": column(L0_conv_bias),
        "beta": column(L1_conv_beta),
        "gammat": np.ascontiguousarray(np.asarray(L1_conv_gamma).T),
    }
    nc = bacc.Bacc("TRN2", target_bir_lowering=False, num_devices=1)
    aps = {n: nc.dram_tensor(f"in_{n}", a.shape, F32, kind="ExternalInput").ap() for n, a in arrays.items()}
    out = nc.dram_tensor("out_y", _OUT, F32, kind="ExternalOutput").ap()
    conv_gdn(nc, out=out, **aps)
    r = run_bass_kernel_spmd(nc, [{f"in_{n}": a for n, a in arrays.items()}], core_ids=[0])
    return r.results[0]["out_y"]
```

```python
from contextlib import ExitStack

import numpy as np

import concourse.bass as bass
from concourse import mybir

F32 = mybir.dt.float32
BF16 = mybir.dt.bfloat16
ALU = mybir.AluOpType
ACT = mybir.ActivationFunctionType
AX = mybir.AxisListType

BN_EPS = 1e-5
OFFSET = 2.0 ** -18
PEDESTAL = OFFSET ** 2
BETA_BOUND = (1e-6 + PEDESTAL) ** 0.5
GAMMA_BOUND = PEDESTAL ** 0.5

ACT_ORDER = (("rsqrt", 0), ("square", 2), ("base", 0), ("rsqrt", 1), ("rsqrt", 2), ("square", 3), ("pool", 0), ("rsqrt", 3), ("pool", 0),
             ("ahead", 0), ("ahead", 1))
ACT_TAPS_ORDER = (("rsqrt", 0), ("square", 2), ("base", 0), ("rsqrt", 1), ("pool", 0), ("rsqrt", 2), ("pool", 0), ("square", 3), ("hidden", 0),
                  ("taps", 0), ("rsqrt", 3), ("ahead", 0), ("ahead", 1))
PE_ORDER = (("den", 0), ("den", 1), ("den", 2), ("next", 0), ("den", 3), ("after", 0))
PE_TAPS_ORDER = (("den", 0), ("den", 1), ("den", 2), ("next", 0), ("hidden", 0), ("taps", 0), ("den", 3), ("after", 0))
SP_ORDER = (("store", 0), ("move", 0), ("store", 1), ("move", 1), ("load", 0), ("store", 2), ("move", 2), ("load", 1), ("store", 3))
LOADS = (((), (5,)), ((0,), (1,)), ((2,), ()), ((3,), (4,)))
LOADS_LATE = ((0, 5),)
PACK = (("w1", 72), ("w2", 384), ("bias", 3), ("bn", 4), ("beta", 1), ("gamma", 96))

SLOTS = 3
QUARTERS = 4
UP_LEFT, UP, UP_RIGHT, LEFT = range(4)
TAPS = 4
TAP_AT = {UP_LEFT: (0, 0), UP: (0, 1), UP_RIGHT: (0, 2), LEFT: (1, 0)}


def conv_gdn(nc, x, par, biasrow, out):
    B, C, H, W = x.shape
    QR = H // QUARTERS
    CD = C // SLOTS
    P = C + CD
    ROWS, COLS = QR + 1, W + 1
    UR = 8
    UNITS = QR // UR
    N = UR * W
    BANK = 512
    G = P // TAPS
    BIAS_PARTS = 3
    CUT = QR // 2
    PIECES = [(h, s) for h in range(2) for s in range(SLOTS)]
    ACT_SLOT, PE_SLOTS = 1, (0, 2)
    CONVS = UNITS * SLOTS
    NORMS = UNITS * QUARTERS
    assert P == 128 and N % BANK == 0 and UNITS % 2 == 0

    ctx = ExitStack()
    with ctx:
        def sb(name, shape, dt=F32):
            return ctx.enter_context(nc.sbuf_tensor(name, shape, dt))

        def sem(name):
            return ctx.enter_context(nc.semaphore(name))

        ximg = sb("ximg", [P, 2, SLOTS, ROWS * COLS])
        y = sb("y", [P, 2, SLOTS, N])
        yd = sb("yd", [C, 2, N])
        sq = sb("sq", [C, QUARTERS, N])
        norm = sb("norm", [C, QUARTERS, N])
        pool_out = sb("pool_out", [P, 2, (QR - CUT + 1) * COLS], BF16)
        part = sb("part", [P, len(PIECES)])
        taps = sb("taps", [P, 2 * SLOTS * TAPS])
        diag = sb("diag", [P, 2, SLOTS, P])
        ident = sb("ident", [P, P])
        hid = sb("hid", [P, TAPS])
        bnw = sb("bnw", [P, 5])
        beta_e = sb("beta_e", [C, 1])
        gam_e = sb("gam_e", [C, C])
        par_s = sb("par_s", [P, par.shape[1]])
        w1r = sb("w1r", [P, SLOTS, TAPS, G])
        bias_f = sb("bias_f", [BIAS_PARTS * 32, 2, SLOTS * P])
        bias_b = sb("bias_b", [BIAS_PARTS * 32, SLOTS * P], BF16)
        bias_p = sb("bias_p", [BIAS_PARTS * 32, SLOTS, P], BF16)
        ones = sb("ones", [BIAS_PARTS * 32, BANK], BF16)
        at = 0
        cols = {}
        for name, n in PACK:
            cols[name] = par_s[:, at:at + n]
            at += n
        w1_s = cols["w1"].rearrange("p (s r) -> p s r", s=SLOTS)
        w2_s = cols["w2"].rearrange("p (s m) -> p s m", s=SLOTS)
        bias_s, bnp, beta_s, gam_s = cols["bias"], cols["bn"], cols["beta"][0:C], cols["gamma"][0:C]
        R = w1_s.shape[2]
        warm = sb("warm", [P, 1])

        acc = ctx.enter_context(nc.psum_tensor("acc", [P, 2, N], F32))
        den = ctx.enter_context(nc.psum_tensor("den", [P, 2, N], F32))
        hid_ps = den[:, 1, 0:1]
        taps_ps = den[:, 1, BANK:BANK + SLOTS * TAPS]

        par_loaded = sem("par_loaded")
        x_loaded = [sem(f"x_loaded{i}") for i in range(len(PIECES))]
        pads_zeroed = sem("pads_zeroed")
        ones_set = sem("ones_set")
        setup = sem("setup")
        setup_own = sem("setup_own")
        bn_root = sem("bn_root")
        consts_ready = sem("consts_ready")
        pooled_act = sem("pooled_act")
        pooled_dve = sem("pooled_dve")
        hid_summed = sem("hid_summed")
        hid_ready = sem("hid_ready")
        taps_summed = sem("taps_summed")
        taps_ready = sem("taps_ready")
        diag_ready = sem("diag_ready")
        ident_ready = sem("ident_ready")
        ident_zeroed = sem("ident_zeroed")
        bias_zeroed = sem("bias_zeroed")
        bias_loaded = sem("bias_loaded")
        bias_split = sem("bias_split")
        based_act = sem("based_act")
        based_pe = sem("based_pe")
        tap_added = sem("tap_added")
        convolved = sem("convolved")
        d_moved = [sem(f"d_moved{i}") for i in range(2)]
        squared = sem("squared")
        summed = sem("summed")
        normed = sem("normed")
        warmed = sem("warmed")
        scaled = sem("scaled")
        stored = [sem(f"stored{g}") for g in range(QUARTERS)]

        def conv_no(b, u, s):
            return b * CONVS + (u * SLOTS + s)

        def norm_no(b, u, g):
            return b * NORMS + (u * QUARTERS + g)

        def unit_no(b, u):
            return b * UNITS + u

        def act_bases(b, u):
            return unit_no(b, u) + 1

        def pe_bases(b, u, s):
            return unit_no(b, u) * len(PE_SLOTS) + PE_SLOTS.index(s) + 1

        def above_zero(n):
            return not isinstance(n, int) or n > 0

        def img(b):
            if isinstance(b, int):
                return ximg[:, b % 2]
            return ximg[:, bass.ds(b % 2, 1)].rearrange("p o s n -> p (o s) n")

        def img_rows(b, s):
            return img(b)[:, s, :].rearrange("p (r c) -> p r c", c=COLS)

        def tap_in(b, u, s, tap):
            r, c = TAP_AT[tap]
            at = (r + u * UR) * COLS + c
            return img(b)[:, s, at:at + UR * COLS].rearrange("p (r c) -> p r c", c=COLS)[:, :, 0:W]

        def tap_w(b, s, tap):
            at = s * TAPS + tap
            if isinstance(b, int):
                at += (b % 2) * SLOTS * TAPS
                return taps[:, at:at + 1]
            return taps[:, bass.ds((b % 2) * (SLOTS * TAPS) + at, 1)]

        def piece_rows(h):
            return (0, CUT) if h == 0 else (CUT, ROWS)

        def in_rows(ap):
            return ap.rearrange("p (r c) -> p r c", c=W)

        def quarter(u, g):
            return y[0:C, u % 2, g] if g < SLOTS else yd[:, u % 2]

        def out_rows(b, u, g):
            r = g * QR + u * UR
            if isinstance(b, int):
                return out[b, :, r:r + UR, :].rearrange("c r w -> c (r w)")
            return out[bass.ds(b, 1), :, r:r + UR, :].rearrange("o c r w -> (o c) (r w)")

        def load_piece(sp, b, i):
            h, s = PIECES[i]
            r0, r1 = piece_rows(h)
            src = x[b] if isinstance(b, int) else x[bass.ds(b, 1)].rearrange("o c h w -> (o c) h w")
            top = max(r0, 1) if s == 0 else r0
            a = s * QR - 1
            sp.dma_start(img_rows(b, s)[0:C, top:r1, 1:COLS], src[:, a + top:a + r1, :]).then_inc(x_loaded[i], 16)
            a = SLOTS * QR - 1
            sp.dma_start(img_rows(b, s)[C:P, r0:r1, 1:COLS],
                         src[s * CD:(s + 1) * CD, a + r0:a + r1, :]).then_inc(x_loaded[i], 16)

        def move_d(sp, b, u, s):
            sp.wait_ge(convolved, conv_no(b, u, s) + 1)
            sp.dma_start(yd[s * CD:(s + 1) * CD, u % 2], y[C:P, u % 2, s]).then_inc(d_moved[u % 2], 16)

        def store(sp, b, u, g):
            sp.wait_ge(scaled, norm_no(b, u, g) + 1)
            sp.dma_start(out_rows(b, u, g), norm[:, g]).then_inc(stored[g], 16)

        def load_next(sp, b, i):
            h, s = PIECES[i]
            sp.wait_ge(convolved, conv_no(b, 2 * h + 1, s) + 1)
            sp.wait_ge(x_loaded[i], 32 * (b + 2))
            load_piece(sp, b + 2, i)

        def sp_unit(sp, b, u):
            nb, nu = (b, u + 1) if u < UNITS - 1 else (b + 1, 0)
            for what, g in SP_ORDER:
                if what == "store":
                    store(sp, b, u, g)
                elif what == "move" and nb < B:
                    move_d(sp, nb, nu, g)
                elif what == "load":
                    for i in LOADS[u][g]:
                        lb = b - 1 if (u, i) in LOADS_LATE else b
                        if 0 <= lb < B - 2:
                            load_next(sp, lb, i)

        def pool_on_act(act, b, i, k):
            h, s = PIECES[i]
            r0, r1 = piece_rows(h)
            r0 = max(r0, 1)
            act.wait_ge(x_loaded[i], 32 * (b + 1))
            src = img(b)[:, s, r0 * COLS:r1 * COLS]
            n = k if isinstance(b, int) and b == 0 else (b - 1) * len(PIECES) + ACT_POOLS + k
            if above_zero(n - 1):
                act.wait_ge(pooled_act, n - 1)
            nc.scalar.activation(pool_out[:, k % 2, 0:(r1 - r0) * COLS], src, ACT.Copy,
                                 accum_out=part[:, i:i + 1]).then_inc(pooled_act, 1)

        def hidden(act, b):
            act.wait_ge(hid_summed, b + 1)
            for t in range(TAPS):
                rows = slice(t * G, (t + 1) * G)
                ins = nc.scalar.activation(hid[rows, t:t + 1], hid_ps[rows], ACT.Relu, bias=bnw[rows, 1:2], scale=bnw[rows, 0:1])
            ins.then_inc(hid_ready, 1)

        def read_taps(act, b):
            act.wait_ge(taps_summed, b + 1)
            if isinstance(b, int):
                dst = taps[:, (b % 2) * SLOTS * TAPS:(b % 2 + 1) * SLOTS * TAPS]
            else:
                dst = taps[:, bass.ds((b % 2) * (SLOTS * TAPS), SLOTS * TAPS)]
            nc.scalar.copy(dst, taps_ps).then_inc(taps_ready, 1)
            act.wait_ge(taps_ready, b + 1)
            for s in PE_SLOTS:
                dst = diag[:, b % 2, s] if isinstance(b, int) else diag[:, bass.ds(b % 2, 1), s].rearrange("p o m -> p (o m)")
                nc.scalar.activation(dst, ident[:, :], ACT.Copy, scale=tap_w(b, s, UP)).then_inc(diag_ready, 1)

        def base(act, b, u, s):
            n = conv_no(b, u, s)
            if above_zero(n - 1):
                act.wait_ge(convolved, n - 1)
            nc.scalar.activation(in_rows(acc[:, n_parity(u, s)]), tap_in(b, u, s, UP), ACT.Identity,
                                 bias=bias_s[:, s:s + 1], scale=tap_w(b, s, UP)).then_inc(based_act, 1)

        def n_parity(u, s):
            return (u * SLOTS + s) % 2

        def square(act, b, u, g):
            if g == 0 and above_zero(norm_no(b, u, 0)):
                act.wait_ge(summed, norm_no(b, u, 0))
            if g < SLOTS:
                act.wait_ge(convolved, conv_no(b, u, g) + 1)
            else:
                act.wait_ge(d_moved[u % 2], d_count(b, u))
            nc.scalar.activation(sq[:, g], quarter(u, g), ACT.Square).then_inc(squared, 1)

        def d_count(b, u):
            return (b * (UNITS // 2) + (u // 2 + 1)) * (16 * SLOTS)

        def rsqrt(act, b, u, g):
            act.wait_ge(summed, norm_no(b, u, g) + 1)
            if above_zero(unit_no(b, u)):
                act.wait_ge(stored[g], unit_no(b, u) * 16)
            nc.scalar.activation(norm[:, g], den[0:C, g % 2], ACT.Abs_reciprocal_sqrt,
                                 bias=beta_e[:, 0:1]).then_inc(normed, 1)

        def act_unit(act, b, u, last):
            nb, nu = (b, u + 1) if u < UNITS - 1 else (b + 1, 0)
            conv = not (last and u == UNITS - 1)
            pool = not last and u < UNITS - 1
            order = ACT_ORDER if not (not last and u == TAPS_UNIT) else ACT_TAPS_ORDER
            piece = 2 * u
            for what, g in order:
                if what == "ahead" and conv:
                    square(act, nb, nu, g)
                elif what == "square":
                    square(act, b, u, g)
                elif what == "rsqrt":
                    rsqrt(act, b, u, g)
                elif what == "base" and conv:
                    base(act, nb, nu, ACT_SLOT)
                elif what == "pool" and pool:
                    pool_on_act(act, b + 1, piece, piece)
                    piece += 1
                elif what == "hidden":
                    hidden(act, b + 1)
                elif what == "taps":
                    read_taps(act, b + 1)

        def hidden_sums(pe, b):
            if b == 0:
                pe.wait_ge(pooled_dve, DVE_POOLS)
                pe.wait_ge(pooled_act, ACT_POOLS)
            else:
                pe.wait_ge(pooled_act, ACT_POOLS + b * len(PIECES))
                pe.wait_ge(normed, norm_no(b - 1, TAPS_UNIT, 1) + 1)
            for i, (h, s) in enumerate(PIECES):
                ins = nc.tensor.matmul(hid_ps, w1r[:, s].rearrange("p t g -> p (t g)"), part[:, i:i + 1],
                                       start=i == 0, stop=i == len(PIECES) - 1)
            ins.then_inc(hid_summed, 1)

        def tap_sums(pe, b):
            pe.wait_ge(hid_ready, b + 1)
            for s in range(SLOTS):
                at = BANK + s * TAPS
                ins = nc.tensor.matmul(den[:, 1, at:at + TAPS], w2_s[:, s], hid[:, :], start=True, stop=True)
            ins.then_inc(taps_summed, 1)

        def base_on_pe(pe, b, u, s):
            n = conv_no(b, u, s)
            pe.wait_ge(diag_ready, b * len(PE_SLOTS) + PE_SLOTS.index(s) + 1)
            if above_zero(n - 1):
                pe.wait_ge(convolved, n - 1)
            rows = BANK // W
            src = tap_in(b, u, s, UP)
            for j in range(N // BANK):
                dst = acc[:, n_parity(u, s), j * BANK:(j + 1) * BANK]
                nc.tensor.matmul(dst, diag[:, b % 2, s], src[:, j * rows:(j + 1) * rows], start=True, stop=False)
                ins = nc.tensor.matmul(dst, bias_p[:, s], ones[:, :], start=False, stop=True)
            ins.then_inc(based_pe, 1)

        def denominators(pe, b, u, g, last=False):
            n = norm_no(b, u, g)
            pe.wait_ge(squared, n + 1)
            if above_zero(n - 1):
                pe.wait_ge(normed, n - 1)
            if not last and (u, g) == (TAPS_UNIT, 3):
                pe.wait_ge(taps_ready, b + 2)
            if n == 1:
                pe.wait_ge(taps_ready, 1)
            for j in range(0, N, BANK):
                ins = nc.tensor.matmul(den[0:C, g % 2, j:j + BANK], gam_e[:, :], sq[:, g, j:j + BANK], start=True, stop=True)
            ins.then_inc(summed, 1)

        def pe_unit(pe, b, u, last):
            nb, nu = (b, u + 1) if u < UNITS - 1 else (b + 1, 0)
            fb, fu = (nb, nu + 1) if nu < UNITS - 1 else (nb + 1, 0)
            for what, g in (PE_ORDER if last or u != TAPS_UNIT else PE_TAPS_ORDER):
                if what == "den":
                    denominators(pe, b, u, g, last)
                elif what == "hidden":
                    hidden_sums(pe, b + 1)
                elif what == "taps":
                    tap_sums(pe, b + 1)
                elif what == "next" and nb < B:
                    base_on_pe(pe, nb, nu, PE_SLOTS[1])
                elif what == "after" and fb < B:
                    base_on_pe(pe, fb, fu, PE_SLOTS[0])

        def n_scaled(b, u, s):
            return norm_no(b, u, s) - 2 * QUARTERS + 1

        def conv(dve, b, u, s):
            n = conv_no(b, u, s)
            a = in_rows(acc[:, n_parity(u, s)])
            if s == ACT_SLOT:
                dve.wait_ge(based_act, act_bases(b, u))
            else:
                dve.wait_ge(based_pe, pe_bases(b, u, s))
            if u == 0 and s == 0:
                dve.wait_ge(taps_ready, b + 1)
            for k, tap in enumerate((UP_LEFT, UP_RIGHT)):
                nc.vector.scalar_tensor_tensor(out=a, in0=tap_in(b, u, s, tap), scalar=tap_w(b, s, tap), in1=a,
                                               op0=ALU.mult, op1=ALU.add).then_inc(tap_added, 1)
                dve.wait_ge(tap_added, 2 * n + (k + 1))
            if unit_no(b, u) >= 2:
                dve.wait_ge(scaled, n_scaled(b, u, s))
                dve.wait_ge(d_moved[u % 2], d_count(b, u) - 16 * SLOTS)
            nc.vector.scalar_tensor_tensor(out=in_rows(y[:, u % 2, s]), in0=tap_in(b, u, s, LEFT), scalar=tap_w(b, s, LEFT),
                                           in1=a, op0=ALU.mult, op1=ALU.add).then_inc(convolved, 1)

        def scale(pool, b, u, g):
            pool.wait_ge(normed, norm_no(b, u, g) + 1)
            if g == SLOTS:
                pool.wait_ge(d_moved[u % 2], d_count(b, u))
            nc.gpsimd.tensor_tensor(norm[:, g], quarter(u, g), norm[:, g], ALU.mult).then_inc(scaled, 1)

        TAPS_UNIT = UNITS - 2
        POOL_ON_ACT = (0, 2, 4, 5)
        POOL_ON_DVE = (1, 3)
        ACT_POOLS, DVE_POOLS = len(POOL_ON_ACT), len(POOL_ON_DVE)
        block = ctx.enter_context(nc.Block())

        @block.sync
        def _(sp):
            sp.wait_ge(pads_zeroed, 1)
            for i in range(len(PIECES)):
                load_piece(sp, 0, i)
            for i in range(len(PIECES)):
                sp.wait_ge(x_loaded[i], 32)
                load_piece(sp, 1, i)
            for s in range(SLOTS):
                move_d(sp, 0, 0, s)
            for b in range(B):
                for u in range(UNITS):
                    sp_unit(sp, b, u)
            for g in range(QUARTERS):
                sp.wait_ge(stored[g], 16 * UNITS * B)

        @block.scalar
        def _(act):
            act.dma_start(par_s[:, :], par[:, :]).then_inc(par_loaded, 16)
            act.wait_ge(bias_zeroed, 1)
            for i in range(BIAS_PARTS):
                act.dma_start(bias_f[32 * i:32 * i + 1, 0], biasrow[:, :]).then_inc(bias_loaded, 16)
            act.wait_ge(ones_set, 1)
            nc.scalar.activation(warm[:, :], warm[:, :], ACT.Abs_reciprocal_sqrt).then_inc(warmed, 1)
            act.wait_ge(setup, 1)
            nc.scalar.activation(bnw[:, 3:4], bnw[:, 2:3], ACT.Abs_reciprocal_sqrt).then_inc(bn_root, 1)
            for k, i in enumerate(POOL_ON_ACT):
                pool_on_act(act, 0, i, k)
            act.wait_ge(consts_ready, 1)
            hidden(act, 0)
            act.wait_ge(ident_ready, 1)
            read_taps(act, 0)
            base(act, 0, 0, ACT_SLOT)
            square(act, 0, 0, 0)
            square(act, 0, 0, 1)
            for u in range(UNITS):
                act_unit(act, 0, u, False)
            with act.Fori(1, B - 1) as b:
                for u in range(UNITS):
                    act_unit(act, b, u, False)
            for u in range(UNITS):
                act_unit(act, B - 1, u, True)

        @block.tensor
        def _(pe):
            pe.wait_ge(consts_ready, 1)
            hidden_sums(pe, 0)
            tap_sums(pe, 0)
            pe.wait_ge(bias_split, 1)
            base_on_pe(pe, 0, 0, PE_SLOTS[0])
            base_on_pe(pe, 0, 0, PE_SLOTS[1])
            base_on_pe(pe, 0, 1, PE_SLOTS[0])
            for b in range(B):
                for u in range(UNITS):
                    pe_unit(pe, b, u, b == B - 1)

        @block.vector
        def _(dve):
            nc.vector.memset(warm[:, :], 1.0).then_inc(ones_set, 1)
            nc.vector.memset(hid[:, :], 0.0)
            nc.vector.memset(w1r[:, :], 0.0)
            nc.vector.memset(ones[:, :], 1.0)
            nc.vector.memset(bias_f[:, :], 0.0).then_inc(bias_zeroed, 1)
            dve.wait_ge(par_loaded, 16)
            nc.vector.tensor_scalar(bnw[:, 2:3], bnp[:, 3:4], BN_EPS, None, ALU.add).then_inc(setup, 1)
            step = [0]

            def chained(ins):
                step[0] += 1
                ins.then_inc(setup_own, 1)
                dve.wait_ge(setup_own, step[0])

            chained(nc.vector.tensor_scalar(gam_s, gam_s, GAMMA_BOUND, None, ALU.max))
            chained(nc.vector.tensor_tensor(gam_e[:, :], gam_s, gam_s, ALU.mult))
            chained(nc.vector.tensor_scalar(gam_e[:, :], gam_e[:, :], PEDESTAL, None, ALU.subtract))
            chained(nc.vector.tensor_scalar(beta_s, beta_s, BETA_BOUND, None, ALU.max))
            chained(nc.vector.tensor_tensor(beta_e[:, :], beta_s, beta_s, ALU.mult))
            chained(nc.vector.tensor_scalar(beta_e[:, :], beta_e[:, :], PEDESTAL, None, ALU.subtract))
            for t in range(TAPS):
                chained(nc.vector.tensor_copy(w1r[:, :, t, 0:R], w1_s))
            dve.wait_ge(bn_root, 1)
            v, r, q = bnw[:, 2:3], bnw[:, 3:4], bnw[:, 4:5]
            for _ in range(2):
                chained(nc.vector.tensor_tensor(q, r, r, ALU.mult))
                chained(nc.vector.tensor_tensor(q, q, v, ALU.mult))
                chained(nc.vector.tensor_scalar(q, q, -0.5, 1.5, ALU.mult, ALU.add))
                chained(nc.vector.tensor_tensor(r, r, q, ALU.mult))
            chained(nc.vector.tensor_tensor(r, r, bnp[:, 0:1], ALU.mult))
            chained(nc.vector.tensor_tensor(q, r, bnp[:, 2:3], ALU.mult))
            chained(nc.vector.tensor_tensor(bnw[:, 1:2], bnp[:, 1:2], q, ALU.subtract))
            nc.vector.tensor_scalar(bnw[:, 0:1], r, 1.0 / (H * W), None, ALU.mult).then_inc(consts_ready, 1)
            dve.wait_ge(bias_loaded, 16 * BIAS_PARTS)
            b_at, rest, part_b = bias_f[:, 0], bias_f[:, 1], bias_b[:, :]
            for i in range(BIAS_PARTS):
                chained(nc.vector.tensor_copy(part_b, b_at))
                row = slice(32 * i, 32 * i + 32)
                chained(nc.vector.tensor_copy(bias_p[row].rearrange("p s m -> p (s m)"), bias_b[row]))
                chained(nc.vector.tensor_tensor(rest, b_at, part_b, ALU.subtract))
                chained(nc.vector.tensor_copy(b_at, rest))
            nc.vector.tensor_copy(rest[:, 0:1], b_at[:, 0:1]).then_inc(bias_split, 1)
            for j in POOL_ON_DVE:
                h, s = PIECES[j]
                r0, r1 = piece_rows(h)
                r0 = max(r0, 1)
                dve.wait_ge(x_loaded[j], 32)
                nc.vector.reduce_sum(part[:, j:j + 1], img(0)[:, s, r0 * COLS:r1 * COLS], AX.X).then_inc(pooled_dve, 1)
            for b in range(B):
                for u in range(UNITS):
                    for s in range(SLOTS):
                        conv(dve, b, u, s)

        @block.gpsimd
        def _(pool):
            nc.gpsimd.memset(ximg[:, :, :, :].rearrange("p b s (r c) -> p (b s r) c", c=COLS)[:, :, 0:1], 0.0)
            nc.gpsimd.memset(ximg[0:C, :, 0, 1:COLS], 0.0).then_inc(pads_zeroed, 1)
            nc.gpsimd.memset(ident[:, :], 0.0).then_inc(ident_zeroed, 1)
            pool.wait_ge(ident_zeroed, 1)
            nc.gpsimd.affine_select(out=ident[:, :], in_=ident[:, :], compare_op=ALU.not_equal, fill=1.0, base=0,
                                    pattern=[[-1, P]], channel_multiplier=1).then_inc(ident_ready, 1)
            with pool.Fori(0, B) as b:
                for u in range(UNITS):
                    for g in range(QUARTERS):
                        scale(pool, b, u, g)


_OUT = (4, 96, 128, 128)


def kernel(x, L0_conv_w1, L0_conv_gamma, L0_conv_beta, L0_conv_running_mean, L0_conv_running_var, L0_conv_w2,
           L0_conv_b2, L0_conv_bias, L1_conv_beta, L1_conv_gamma):
    import concourse.bacc as bacc
    from concourse.bass_utils import run_bass_kernel_spmd

    w1t, w2, gammat = np.asarray(L0_conv_w1).T, np.asarray(L0_conv_w2), np.asarray(L1_conv_gamma).T
    C, R = w1t.shape
    CD, G, taps = C // SLOTS, 128 // TAPS, w2.reshape(C, -1, R)

    def by_slots(a):
        return np.stack([np.concatenate([a, a[s * CD:(s + 1) * CD]]) for s in range(SLOTS)], 1)

    w2_rows = np.zeros((TAPS, G, C), np.float32)
    w2_rows[:, :R] = taps[:, :TAPS].transpose(1, 2, 0)
    w2_rows[:, R] = np.asarray(L0_conv_b2).reshape(C, -1)[:, :TAPS].T
    bn = np.zeros((TAPS, G, 4), np.float32)
    for i, a in enumerate((L0_conv_gamma, L0_conv_beta, L0_conv_running_mean, L0_conv_running_var)):
        bn[:, :R, i] = np.asarray(a)
    bn[:, R, 1] = 1.0
    bias = by_slots(np.asarray(L0_conv_bias).reshape(-1, 1))
    fields = {
        "w1": by_slots(w1t).reshape(128, -1),
        "w2": by_slots(w2_rows.reshape(128, C).T).transpose(2, 1, 0).reshape(128, -1),
        "bias": bias.reshape(128, SLOTS),
        "bn": bn.reshape(128, 4),
        "beta": np.pad(np.asarray(L1_conv_beta).reshape(-1, 1), ((0, CD), (0, 0))),
        "gamma": np.pad(gammat, ((0, CD), (0, 0))),
    }
    arrays = {
        "x": np.ascontiguousarray(x),
        "par": np.ascontiguousarray(np.concatenate([fields[name] for name, _ in PACK], 1)),
        "biasrow": np.ascontiguousarray(bias.reshape(128, SLOTS).T.reshape(1, -1)),
    }
    nc = bacc.Bacc("TRN2", target_bir_lowering=False, num_devices=1)
    aps = {n: nc.dram_tensor(f"in_{n}", a.shape, F32, kind="ExternalInput").ap() for n, a in arrays.items()}
    out = nc.dram_tensor("out_y", _OUT, F32, kind="ExternalOutput").ap()
    conv_gdn(nc, out=out, **aps)
    r = run_bass_kernel_spmd(nc, [{f"in_{n}": a for n, a in arrays.items()}], core_ids=[0])
    return r.results[0]["out_y"]
```

```python
from contextlib import ExitStack

import numpy as np

import concourse.bass as bass
from concourse import mybir

F32 = mybir.dt.float32
BF16 = mybir.dt.bfloat16
ALU = mybir.AluOpType
ACT = mybir.ActivationFunctionType
AX = mybir.AxisListType

BN_EPS = 1e-5
OFFSET = 2.0 ** -18
PEDESTAL = OFFSET ** 2
BETA_BOUND = (1e-6 + PEDESTAL) ** 0.5
GAMMA_BOUND = PEDESTAL ** 0.5


def steps(text):
    names = [(word.rstrip("0123456789"), word) for word in text.split()]
    return tuple((name, int(word[len(name):] or 0)) for name, word in names)


ACT_STEPS = tuple(map(steps, (
    "square2 rsqrt0 base1 rsqrt1 ahead0 rsqrt2 pool2 pool3 rsqrt3 ahead1",
    "square2 rsqrt0 base1 ahead0 rsqrt1 pool4 rsqrt2 pool5 ahead1 rsqrt3",
    "square2 rsqrt0 base1 rsqrt1 hidden rsqrt2 ahead0 ahead1 taps first rsqrt3",
    "square2 rsqrt0 base1 rsqrt1 pool0 rsqrt2 ahead0 pool1 ahead1 rsqrt3")))
PE_STEPS = tuple(map(steps, (
    "den0 den1 den2 next den3 after",
    "den0 den1 den2 next den3 after",
    "den0 den1 den2 hidden next taps den3",
    "den0 den1 den2 next den3 after")))
SP_STEPS = tuple(map(steps, (
    "move0 store0 move1 move2 store1 store2 late5 store3",
    "move0 store0 store1 move1 load0 move2 store2 store3 load1",
    "store0 move0 load2 store1 move1 store2 move2 store3",
    "move0 store0 load3 move1 store1 store2 move2 store3 load4")))
LAST_SP_STEPS = steps("store0 move0 store1 move1 move2 store2 store3")
POOL_STEPS = tuple(map(steps, (
    "scale0 square3 scale1 scale2 scale3",
    "scale0 square3 scale1 scale2 scale3",
    "parts scale0 square3 scale1 scale2 scale3",
    "scale0 square3 scale1 scale2 scale3")))

SLOTS = 3
QUARTERS = 4
UP_LEFT, UP, UP_RIGHT, LEFT = range(4)
TAPS = 4
TAP_AT = {UP_LEFT: (0, 0), UP: (0, 1), UP_RIGHT: (0, 2), LEFT: (1, 0)}


def conv_gdn(nc, x, par, biasrow, out, widths):
    B, C, H, W = x.shape
    QR = H // QUARTERS
    CD = C // SLOTS
    P = C + CD
    ROWS, COLS = QR + 1, W + 1
    UR = 8
    UNITS = QR // UR
    N = UR * W
    BANK = 512
    G = P // TAPS
    BIAS_PARTS = 3
    CUT = QR // 2
    PIECES = [(h, s) for h in range(2) for s in range(SLOTS)]
    ACT_SLOT, PE_SLOTS = 1, (0, 2)
    CONVS = UNITS * SLOTS
    NORMS = UNITS * QUARTERS
    HALVES = (slice(0, N // 2), slice(N // 2, N))
    TAPS_UNIT = UNITS - 2
    LAST_PIECE = len(PIECES) - 1
    POOL_ON_ACT = ((0, "all"), (2, "all"), (4, "all"), (LAST_PIECE, "top"))
    POOL_ON_DVE = ((1, "all"), (3, "all"), (LAST_PIECE, "end"))
    ACT_POOLS = len(POOL_ON_ACT)
    WAKING = 6
    BLOCKS = [(b, u, s) for b in range(B) for u in range(UNITS) for s in range(SLOTS)]
    assert P == 128 and N % BANK == 0 and UNITS % 2 == 0

    ctx = ExitStack()
    with ctx:
        def sb(name, shape, dt=F32):
            return ctx.enter_context(nc.sbuf_tensor(name, shape, dt))

        def sem(name):
            return ctx.enter_context(nc.semaphore(name))

        ximg = sb("ximg", [P, 2, SLOTS, ROWS * COLS])
        y = sb("y", [P, 2, SLOTS, N])
        yd = sb("yd", [C, 2, N])
        sq = sb("sq", [C, QUARTERS, N])
        norm = sb("norm", [C, QUARTERS, N])
        pool_out = sb("pool_out", [P, 2, (QR - CUT + 1) * COLS], BF16)
        part = sb("part", [P, len(PIECES) + 1])
        part_x = sb("part_x", [P, SLOTS])
        taps = sb("taps", [P, 2 * SLOTS * TAPS])
        diag = sb("diag", [P, 2, SLOTS, P])
        ident = sb("ident", [P, P])
        hid = sb("hid", [P, TAPS])
        bnw = sb("bnw", [P, 6])
        own_tap = sb("own_tap", [P, TAPS])
        beta_e = sb("beta_e", [C, 1])
        gam_e = sb("gam_e", [C, C])
        par_s = sb("par_s", [P, par.shape[1]])
        w1r = sb("w1r", [P, SLOTS, TAPS, G])
        bias_f = sb("bias_f", [BIAS_PARTS * 32, 2, SLOTS * P])
        bias_b = sb("bias_b", [BIAS_PARTS * 32, SLOTS * P], BF16)
        bias_p = sb("bias_p", [BIAS_PARTS * 32, SLOTS, P], BF16)
        ones = sb("ones", [BIAS_PARTS * 32, BANK], BF16)
        warm = sb("warm", [P, 1])
        at = 0
        cols = {}
        for name, n in widths:
            cols[name] = par_s[:, at:at + n]
            at += n
        w1_s = cols["w1"].rearrange("p (s r) -> p s r", s=SLOTS)
        w2_s = cols["w2"].rearrange("p (s m) -> p s m", s=SLOTS)
        bias_s, bnp, beta_s, gam_s = cols["bias"], cols["bn"], cols["beta"][0:C], cols["gamma"][0:C]
        R = w1_s.shape[2]

        acc = ctx.enter_context(nc.psum_tensor("acc", [P, 2, N], F32))
        den = ctx.enter_context(nc.psum_tensor("den", [P, 2, N], F32))
        hid_ps = den[:, 1, 0:1]
        taps_ps = den[:, 1, BANK:BANK + SLOTS * TAPS]

        par_loaded = sem("par_loaded")
        bias_loaded = sem("bias_loaded")
        x_loaded = [sem(f"x_loaded{i}") for i in range(len(PIECES))]
        pads_zeroed = sem("pads_zeroed")
        warm_set = sem("warm_set")
        warmed = sem("warmed")
        bias_zeroed = sem("bias_zeroed")
        ident_zeroed = sem("ident_zeroed")
        ident_ready = sem("ident_ready")
        own_tap_written = sem("own_tap_written")
        var_ready = sem("var_ready")
        bn_root = sem("bn_root")
        const_step = sem("const_step")
        consts_ready = sem("consts_ready")
        bias_split = sem("bias_split")
        pooled_act = sem("pooled_act")
        pooled_dve = sem("pooled_dve")
        halves_added = sem("halves_added")
        hid_summed = sem("hid_summed")
        hid_normed = sem("hid_normed")
        hid_ready = sem("hid_ready")
        taps_summed = sem("taps_summed")
        taps_ready = sem("taps_ready")
        diag_ready = sem("diag_ready")
        based_act = sem("based_act")
        based_pe = sem("based_pe")
        tap_added = sem("tap_added")
        convolved = sem("convolved")
        d_moved = [sem(f"d_moved{i}") for i in range(2)]
        squared = sem("squared")
        squared_d = sem("squared_d")
        summed = sem("summed")
        normed = sem("normed")
        scaled = sem("scaled")
        stored = [sem(f"stored{g}") for g in range(QUARTERS)]
        last_squared = sem("last_squared")
        last_summed = sem("last_summed")
        last_normed = sem("last_normed")
        last_scaled = sem("last_scaled")

        def conv_no(b, u, s):
            return b * CONVS + (u * SLOTS + s)

        def norm_no(b, u, g):
            return b * NORMS + (u * QUARTERS + g)

        def unit_no(b, u):
            return b * UNITS + u

        def d_count(b, u):
            return (b * (UNITS // 2) + (u // 2 + 1)) * (16 * SLOTS)

        def n_scaled(b, u, s):
            return norm_no(b, u, s) - 2 * QUARTERS + 1

        def on_act(b, u, s):
            return s == ACT_SLOT or (u, s) == (0, 0) or (b, u) == (0, 0)

        def bases(b, u, s):
            here = on_act(b, u, s)
            return sum(on_act(*block_n) == here for block_n in BLOCKS[:conv_no(b, u, s) + 1])

        def above_zero(n):
            return not isinstance(n, int) or n > 0

        def img(b):
            if isinstance(b, int):
                return ximg[:, b % 2]
            return ximg[:, bass.ds(b % 2, 1)].rearrange("p o s n -> p (o s) n")

        def img_rows(b, s):
            return img(b)[:, s, :].rearrange("p (r c) -> p r c", c=COLS)

        def tap_in(b, u, s, tap):
            r, c = TAP_AT[tap]
            at = (r + u * UR) * COLS + c
            return img(b)[:, s, at:at + UR * COLS].rearrange("p (r c) -> p r c", c=COLS)[:, :, 0:W]

        def tap_w(b, s, tap):
            at = s * TAPS + tap
            if isinstance(b, int):
                at += (b % 2) * SLOTS * TAPS
                return taps[:, at:at + 1]
            return taps[:, bass.ds((b % 2) * (SLOTS * TAPS) + at, 1)]

        def piece_rows(h):
            return (0, CUT) if h == 0 else (CUT, ROWS)

        def sums(u, s):
            return acc[:, (u * SLOTS + s) % 2]

        def in_rows(ap):
            return ap.rearrange("p (r c) -> p r c", c=W)

        def quarter(u, g):
            return y[0:C, u % 2, g] if g < SLOTS else yd[:, u % 2]

        def out_rows(b, u, g):
            r = g * QR + u * UR
            return out[b, :, r:r + UR, :].rearrange("c r w -> c (r w)")

        def load_piece(sp, b, i):
            h, s = PIECES[i]
            r0, r1 = piece_rows(h)
            top = max(r0, 1) if s == 0 else r0
            a = s * QR - 1
            sp.dma_start(img_rows(b, s)[0:C, top:r1, 1:COLS], x[b, :, a + top:a + r1, :]).then_inc(x_loaded[i], 16)
            a = SLOTS * QR - 1
            sp.dma_start(img_rows(b, s)[C:P, r0:r1, 1:COLS],
                         x[b, s * CD:(s + 1) * CD, a + r0:a + r1, :]).then_inc(x_loaded[i], 16)

        def move_d(sp, b, u, s):
            sp.wait_ge(convolved, conv_no(b, u, s) + 1)
            sp.dma_start(yd[s * CD:(s + 1) * CD, u % 2], y[C:P, u % 2, s]).then_inc(d_moved[u % 2], 16)

        def store(sp, b, u, g):
            sp.wait_ge(scaled, norm_no(b, u, g) + 1)
            sp.dma_start(out_rows(b, u, g), norm[:, g]).then_inc(stored[g], 16)

        def last_stores(sp):
            for g in range(SLOTS):
                sp.wait_ge(last_scaled, g + 1)
                sp.dma_start(out_rows(B - 1, UNITS - 1, g), norm[:, g]).then_inc(stored[g], 16)
            for h, cols in enumerate(HALVES):
                sp.wait_ge(last_scaled, SLOTS + h + 1)
                sp.dma_start(out_rows(B - 1, UNITS - 1, SLOTS)[:, cols], norm[:, SLOTS, cols]).then_inc(stored[SLOTS], 16)

        def load_next(sp, b, i):
            h, s = PIECES[i]
            sp.wait_ge(convolved, conv_no(b, 2 * h + 1, s) + 1)
            sp.wait_ge(x_loaded[i], 32 * (b + 2))
            load_piece(sp, b + 2, i)

        def sp_unit(sp, b, u):
            nb, nu = (b, u + 1) if u < UNITS - 1 else (b + 1, 0)
            for what, g in LAST_SP_STEPS if (b, u) == (B - 1, UNITS - 2) else SP_STEPS[u]:
                if what == "store":
                    store(sp, b, u, g)
                elif what == "move" and nb < B:
                    move_d(sp, nb, nu, g)
                elif what in ("load", "late"):
                    lb = b - 1 if what == "late" else b
                    if 0 <= lb < B - 2:
                        load_next(sp, lb, g)

        def first_rows(i, part_of):
            r0, r1 = piece_rows(PIECES[i][0])
            r0, mid = max(r0, 1), (r0 + r1) // 2
            return {"all": (r0, r1), "top": (r0, mid), "end": (mid, r1)}[part_of]

        def first_pool(engine, i, part_of):
            r0, r1 = first_rows(i, part_of)
            engine.wait_ge(x_loaded[i], 32)
            src = img(0)[:, PIECES[i][1], r0 * COLS:r1 * COLS]
            col = len(PIECES) if part_of == "end" else i
            if engine is nc.vector:
                nc.vector.reduce_sum(part[:, col:col + 1], src, AX.X).then_inc(pooled_dve, 1)
            else:
                k = [p[0] for p in POOL_ON_ACT].index(i)
                if k > 1:
                    engine.wait_ge(pooled_act, k - 1)
                nc.scalar.activation(pool_out[:, k % 2, 0:(r1 - r0) * COLS], src, ACT.Copy,
                                     accum_out=part[:, col:col + 1]).then_inc(pooled_act, 1)

        def pool_on_act(act, b, i, k):
            h, s = PIECES[i]
            r0, r1 = piece_rows(h)
            r0 = max(r0, 1)
            act.wait_ge(x_loaded[i], 32 * (b + 1))
            src = img(b)[:, s, r0 * COLS:r1 * COLS]
            n = (b - 1) * len(PIECES) + ACT_POOLS + k
            act.wait_ge(pooled_act, n - 1)
            nc.scalar.activation(pool_out[:, k % 2, 0:(r1 - r0) * COLS], src, ACT.Copy,
                                 accum_out=part[:, i:i + 1]).then_inc(pooled_act, 1)

        def hidden(act, b):
            act.wait_ge(hid_summed, b + 1)
            nc.scalar.activation(bnw[:, 5:6], hid_ps, ACT.Identity, bias=bnw[:, 1:2],
                                 scale=bnw[:, 0:1]).then_inc(hid_normed, 1)
            act.wait_ge(hid_normed, b + 1)
            nc.scalar.activation(hid[:, :], own_tap[:, :], ACT.Relu, scale=bnw[:, 5:6]).then_inc(hid_ready, 1)

        def read_taps(act, b):
            act.wait_ge(taps_summed, b + 1)
            if isinstance(b, int):
                dst = taps[:, (b % 2) * SLOTS * TAPS:(b % 2 + 1) * SLOTS * TAPS]
            else:
                dst = taps[:, bass.ds((b % 2) * (SLOTS * TAPS), SLOTS * TAPS)]
            nc.scalar.copy(dst, taps_ps).then_inc(taps_ready, 1)
            act.wait_ge(taps_ready, b + 1)

        def diagonal(act, b, s):
            dst = diag[:, b % 2, s] if isinstance(b, int) else diag[:, bass.ds(b % 2, 1), s].rearrange("p o m -> p (o m)")
            nc.scalar.activation(dst, ident[:, :], ACT.Copy, scale=tap_w(b, s, UP)).then_inc(diag_ready, 1)

        def base(act, b, u, s):
            n = conv_no(b, u, s)
            if above_zero(n - 1):
                act.wait_ge(convolved, n - 1)
            nc.scalar.activation(in_rows(sums(u, s)), tap_in(b, u, s, UP), ACT.Identity,
                                 bias=bias_s[:, s:s + 1], scale=tap_w(b, s, UP)).then_inc(based_act, 1)

        def square(act, b, u, g):
            if above_zero(unit_no(b, u)):
                act.wait_ge(summed, norm_no(b, u, g) - QUARTERS + 1)
            act.wait_ge(convolved, conv_no(b, u, g) + 1)
            nc.scalar.activation(sq[:, g], quarter(u, g), ACT.Square).then_inc(squared, 1)

        def last_squares_d(act):
            act.wait_ge(d_moved[(UNITS - 1) % 2], d_count(B - 1, UNITS - 1))
            for cols in HALVES:
                nc.scalar.activation(sq[:, SLOTS, cols], quarter(UNITS - 1, SLOTS)[:, cols],
                                     ACT.Square).then_inc(last_squared, 1)

        def last_rsqrts_d(act):
            act.wait_ge(stored[SLOTS], unit_no(B - 1, UNITS - 1) * 16)
            for h, cols in enumerate(HALVES):
                act.wait_ge(last_summed, h + 1)
                nc.scalar.activation(norm[:, SLOTS, cols], den[0:C, 1, cols], ACT.Abs_reciprocal_sqrt,
                                     bias=beta_e[:, 0:1]).then_inc(last_normed, 1)

        def rsqrt(act, b, u, g):
            act.wait_ge(summed, norm_no(b, u, g) + 1)
            if above_zero(unit_no(b, u)):
                act.wait_ge(stored[g], unit_no(b, u) * 16)
            nc.scalar.activation(norm[:, g], den[0:C, g % 2], ACT.Abs_reciprocal_sqrt,
                                 bias=beta_e[:, 0:1]).then_inc(normed, 1)

        def act_unit(act, b, u, last, pools):
            nb, nu = (b, u + 1) if u < UNITS - 1 else (b + 1, 0)
            for what, g in ACT_STEPS[u]:
                if what == "ahead":
                    square(act, nb, nu, g)
                elif what == "square":
                    square(act, b, u, g)
                elif what == "rsqrt":
                    rsqrt(act, b, u, g)
                elif what == "base":
                    base(act, nb, nu, g)
                elif what == "first" and not last:
                    base(act, b + 1, 0, 0)
                elif what == "pool" and pools:
                    pool_on_act(act, b + 2 if u == UNITS - 1 else b + 1, g, g)
                elif last:
                    continue
                elif what == "hidden":
                    hidden(act, b + 1)
                elif what == "taps":
                    read_taps(act, b + 1)
                    for s in PE_SLOTS:
                        diagonal(act, b + 1, s)

        def hidden_sum(s, sums, first, last):
            return nc.tensor.matmul(hid_ps, w1r[:, s].rearrange("p t g -> p (t g)"), sums,
                                    start=first, stop=last)

        def first_hidden_sums(pe):
            end = len(PIECES)
            order = ((0, pooled_act, 1), (2, pooled_act, 2), (1, pooled_dve, 1), (4, pooled_act, 3),
                     (3, pooled_dve, 2), (LAST_PIECE, pooled_act, 4), (end, pooled_dve, 3))
            for k, (i, pooled, n) in enumerate(order):
                pe.wait_ge(pooled, n)
                ins = hidden_sum(PIECES[min(i, LAST_PIECE)][1], part[:, i:i + 1], k == 0, k == len(order) - 1)
                if k == 2:
                    for _ in range(WAKING):
                        nc.tensor.matmul(den[:, 0, 0:BANK], bias_p[:, 0], ones[:, :], start=True, stop=True)
            ins.then_inc(hid_summed, 1)

        def hidden_sums(pe, b):
            pe.wait_ge(halves_added, b)
            pe.wait_ge(normed, norm_no(b - 1, TAPS_UNIT, 1) + 1)
            for s in range(SLOTS):
                ins = hidden_sum(s, part_x[:, s:s + 1], s == 0, s == SLOTS - 1)
            ins.then_inc(hid_summed, 1)

        def tap_sums(pe, b):
            pe.wait_ge(hid_ready, b + 1)
            for s in range(SLOTS):
                at = BANK + s * TAPS
                ins = nc.tensor.matmul(den[:, 1, at:at + TAPS], w2_s[:, s], hid[:, :], start=True, stop=True)
            ins.then_inc(taps_summed, 1)

        def base_on_pe(pe, b, u, s):
            n = conv_no(b, u, s)
            pe.wait_ge(diag_ready, b * len(PE_SLOTS) + PE_SLOTS.index(s) + 1)
            if above_zero(n - 1):
                pe.wait_ge(convolved, n - 1)
            rows = BANK // W
            src = tap_in(b, u, s, UP)
            for j in range(N // BANK):
                dst = sums(u, s)[:, j * BANK:(j + 1) * BANK]
                nc.tensor.matmul(dst, diag[:, b % 2, s], src[:, j * rows:(j + 1) * rows], start=True, stop=False)
                ins = nc.tensor.matmul(dst, bias_p[:, s], ones[:, :], start=False, stop=True)
            ins.then_inc(based_pe, 1)

        def denominators(pe, b, u, g, last):
            n = norm_no(b, u, g)
            if g < SLOTS:
                pe.wait_ge(squared, unit_no(b, u) * SLOTS + g + 1)
            else:
                pe.wait_ge(squared_d, unit_no(b, u) + 1)
            if above_zero(n - 1):
                pe.wait_ge(normed, n - 1)
            if not last and (u, g) == (TAPS_UNIT, SLOTS):
                pe.wait_ge(taps_ready, b + 2)
            if n == 1:
                pe.wait_ge(taps_ready, 1)
            for j in range(0, N, BANK):
                ins = nc.tensor.matmul(den[0:C, g % 2, j:j + BANK], gam_e[:, :], sq[:, g, j:j + BANK], start=True, stop=True)
            ins.then_inc(summed, 1)

        def last_denominators(pe):
            pe.wait_ge(normed, norm_no(B - 1, UNITS - 1, 1) + 1)
            for h, cols in enumerate(HALVES):
                pe.wait_ge(last_squared, h + 1)
                nc.tensor.matmul(den[0:C, 1, cols], gam_e[:, :], sq[:, SLOTS, cols],
                                 start=True, stop=True).then_inc(last_summed, 1)

        def pe_unit(pe, b, u, last):
            nb, nu = (b, u + 1) if u < UNITS - 1 else (b + 1, 0)
            fb, fu = (nb, nu + 1) if nu < UNITS - 1 else (nb + 1, 0)
            for what, g in PE_STEPS[u]:
                if what == "den" and (b, u, g) == (B - 1, UNITS - 1, SLOTS):
                    last_denominators(pe)
                elif what == "den":
                    denominators(pe, b, u, g, last)
                elif what == "hidden" and not last:
                    hidden_sums(pe, b + 1)
                elif what == "taps" and not last:
                    tap_sums(pe, b + 1)
                elif what == "next" and nb < B:
                    base_on_pe(pe, nb, nu, PE_SLOTS[1])
                elif what == "after" and fb < B:
                    base_on_pe(pe, fb, fu, PE_SLOTS[0])

        def conv(dve, b, u, s):
            n, a = conv_no(b, u, s), in_rows(sums(u, s))
            dve.wait_ge(based_act if on_act(b, u, s) else based_pe, bases(b, u, s))
            if (u, s) == (0, 0):
                dve.wait_ge(taps_ready, b + 1)
            for k, tap in enumerate((UP_LEFT, UP_RIGHT)):
                nc.vector.scalar_tensor_tensor(out=a, in0=tap_in(b, u, s, tap), scalar=tap_w(b, s, tap),
                                               in1=a, op0=ALU.mult, op1=ALU.add).then_inc(tap_added, 1)
                dve.wait_ge(tap_added, 2 * n + (k + 1))
            if unit_no(b, u) >= 2:
                dve.wait_ge(scaled, n_scaled(b, u, s))
                dve.wait_ge(d_moved[u % 2], d_count(b, u) - 16 * SLOTS)
            nc.vector.scalar_tensor_tensor(out=in_rows(y[:, u % 2, s]), in0=tap_in(b, u, s, LEFT), scalar=tap_w(b, s, LEFT),
                                           in1=a, op0=ALU.mult, op1=ALU.add).then_inc(convolved, 1)

        def square_d(pool, b, u):
            pool.wait_ge(d_moved[u % 2], d_count(b, u))
            nc.gpsimd.tensor_tensor(sq[:, SLOTS], quarter(u, SLOTS), quarter(u, SLOTS), ALU.mult).then_inc(squared_d, 1)

        def add_halves(pool, b):
            pool.wait_ge(pooled_act, b * len(PIECES) + ACT_POOLS)
            nc.gpsimd.tensor_tensor(part_x[:, :], part[:, 0:SLOTS], part[:, SLOTS:2 * SLOTS],
                                    ALU.add).then_inc(halves_added, 1)

        def scale(pool, b, u, g):
            pool.wait_ge(normed, norm_no(b, u, g) + 1)
            nc.gpsimd.tensor_tensor(norm[:, g], quarter(u, g), norm[:, g], ALU.mult).then_inc(scaled, 1)

        def pool_unit(pool, b, u, last):
            for what, g in POOL_STEPS[u]:
                if what == "parts":
                    if not last:
                        add_halves(pool, b + 1)
                elif what == "scale":
                    scale(pool, b, u, g)
                else:
                    square_d(pool, b, u)

        block = ctx.enter_context(nc.Block())

        @block.sync
        def _(sp):
            sp.wait_ge(pads_zeroed, 1)
            for i in range(len(PIECES)):
                load_piece(sp, 0, i)
            for i in range(len(PIECES)):
                sp.wait_ge(x_loaded[i], 32)
                load_piece(sp, 1, i)
            for s in range(SLOTS):
                move_d(sp, 0, 0, s)
            for b in range(B):
                for u in range(UNITS - 1 if b == B - 1 else UNITS):
                    sp_unit(sp, b, u)
            last_stores(sp)
            for g in range(QUARTERS):
                sp.wait_ge(stored[g], 16 * (UNITS * B + (1 if g == SLOTS else 0)))

        @block.scalar
        def _(act):
            act.dma_start(par_s[:, :], par[:, :]).then_inc(par_loaded, 16)
            act.wait_ge(bias_zeroed, 1)
            for i in range(BIAS_PARTS):
                act.dma_start(bias_f[32 * i:32 * i + 1, 0], biasrow[:, :]).then_inc(bias_loaded, 16)
            act.wait_ge(warm_set, 1)
            nc.scalar.activation(warm[:, :], warm[:, :], ACT.Abs_reciprocal_sqrt).then_inc(warmed, 1)
            act.wait_ge(var_ready, 1)
            nc.scalar.activation(bnw[:, 3:4], bnw[:, 2:3], ACT.Abs_reciprocal_sqrt).then_inc(bn_root, 1)
            for i, part_of in POOL_ON_ACT:
                first_pool(act, i, part_of)
            act.wait_ge(own_tap_written, TAPS + 1)
            act.wait_ge(consts_ready, 1)
            hidden(act, 0)
            act.wait_ge(ident_ready, 1)
            read_taps(act, 0)
            for s in range(SLOTS):
                base(act, 0, 0, s)
            for s in PE_SLOTS:
                diagonal(act, 0, s)
            pool_on_act(act, 1, 0, 0)
            pool_on_act(act, 1, 1, 1)
            square(act, 0, 0, 0)
            square(act, 0, 0, 1)
            for u in range(UNITS - 1):
                act_unit(act, 0, u, False, True)
            with act.Fori(1, B - 1) as b:
                act_unit(act, b - 1, UNITS - 1, False, True)
                for u in range(UNITS - 1):
                    act_unit(act, b, u, False, True)
            act_unit(act, B - 2, UNITS - 1, False, False)
            for u in range(UNITS - 1):
                act_unit(act, B - 1, u, True, False)
            square(act, B - 1, UNITS - 1, 2)
            rsqrt(act, B - 1, UNITS - 1, 0)
            rsqrt(act, B - 1, UNITS - 1, 1)
            last_squares_d(act)
            rsqrt(act, B - 1, UNITS - 1, 2)
            last_rsqrts_d(act)

        @block.tensor
        def _(pe):
            pe.wait_ge(consts_ready, 1)
            pe.wait_ge(bias_split, 1)
            first_hidden_sums(pe)
            tap_sums(pe, 0)
            base_on_pe(pe, 0, 1, PE_SLOTS[0])
            for b in range(B):
                for u in range(UNITS):
                    pe_unit(pe, b, u, b == B - 1)

        @block.vector
        def _(dve):
            nc.vector.memset(warm[:, :], 1.0).then_inc(warm_set, 1)
            nc.vector.memset(w1r[:, :], 0.0)
            nc.vector.memset(ones[:, :], 1.0)
            nc.vector.memset(bias_f[:, :], 0.0).then_inc(bias_zeroed, 1)
            dve.wait_ge(par_loaded, 16)
            nc.vector.tensor_scalar(bnw[:, 2:3], bnp[:, 3:4], BN_EPS, None, ALU.add).then_inc(var_ready, 1)
            step = [0]

            def chained(ins):
                step[0] += 1
                ins.then_inc(const_step, 1)
                dve.wait_ge(const_step, step[0])

            chained(nc.vector.tensor_scalar(gam_s, gam_s, GAMMA_BOUND, None, ALU.max))
            chained(nc.vector.tensor_tensor(gam_e[:, :], gam_s, gam_s, ALU.mult))
            chained(nc.vector.tensor_scalar(gam_e[:, :], gam_e[:, :], PEDESTAL, None, ALU.subtract))
            chained(nc.vector.tensor_scalar(beta_s, beta_s, BETA_BOUND, None, ALU.max))
            chained(nc.vector.tensor_tensor(beta_e[:, :], beta_s, beta_s, ALU.mult))
            chained(nc.vector.tensor_scalar(beta_e[:, :], beta_e[:, :], PEDESTAL, None, ALU.subtract))
            for t in range(TAPS):
                chained(nc.vector.tensor_copy(w1r[:, :, t, 0:R], w1_s))
            dve.wait_ge(bn_root, 1)
            v, r, q = bnw[:, 2:3], bnw[:, 3:4], bnw[:, 4:5]
            for _ in range(2):
                chained(nc.vector.tensor_tensor(q, r, r, ALU.mult))
                chained(nc.vector.tensor_tensor(q, q, v, ALU.mult))
                chained(nc.vector.tensor_scalar(q, q, -0.5, 1.5, ALU.mult, ALU.add))
                chained(nc.vector.tensor_tensor(r, r, q, ALU.mult))
            chained(nc.vector.tensor_tensor(r, r, bnp[:, 0:1], ALU.mult))
            chained(nc.vector.tensor_tensor(q, r, bnp[:, 2:3], ALU.mult))
            chained(nc.vector.tensor_tensor(bnw[:, 1:2], bnp[:, 1:2], q, ALU.subtract))
            nc.vector.tensor_scalar(bnw[:, 0:1], r, 1.0 / (H * W), None, ALU.mult).then_inc(consts_ready, 1)
            dve.wait_ge(bias_loaded, 16 * BIAS_PARTS)
            b_at, rest, part_b = bias_f[:, 0], bias_f[:, 1], bias_b[:, :]
            for i in range(BIAS_PARTS):
                chained(nc.vector.tensor_copy(part_b, b_at))
                row = slice(32 * i, 32 * i + 32)
                ins = nc.vector.tensor_copy(bias_p[row].rearrange("p s m -> p (s m)"), bias_b[row])
                if i < BIAS_PARTS - 1:
                    chained(ins)
                    chained(nc.vector.tensor_tensor(rest, b_at, part_b, ALU.subtract))
                    chained(nc.vector.tensor_copy(b_at, rest))
            ins.then_inc(bias_split, 1)
            for i, part_of in POOL_ON_DVE:
                first_pool(dve, i, part_of)
            for b, u, s in BLOCKS:
                conv(dve, b, u, s)
            u = UNITS - 1
            for g in range(SLOTS):
                dve.wait_ge(normed, norm_no(B - 1, u, g) + 1)
                nc.vector.tensor_tensor(norm[:, g], quarter(u, g), norm[:, g], ALU.mult).then_inc(last_scaled, 1)
            dve.wait_ge(d_moved[u % 2], d_count(B - 1, u))
            for h, cols in enumerate(HALVES):
                dve.wait_ge(last_normed, h + 1)
                nc.vector.tensor_tensor(norm[:, SLOTS, cols], quarter(u, SLOTS)[:, cols], norm[:, SLOTS, cols],
                                        ALU.mult).then_inc(last_scaled, 1)

        @block.gpsimd
        def _(pool):
            nc.gpsimd.memset(ximg[:, :, :, :].rearrange("p b s (r c) -> p (b s r) c", c=COLS)[:, :, 0:1], 0.0)
            nc.gpsimd.memset(ximg[0:C, :, 0, 1:COLS], 0.0).then_inc(pads_zeroed, 1)
            nc.gpsimd.memset(ident[:, :], 0.0).then_inc(ident_zeroed, 1)
            nc.gpsimd.memset(own_tap[:, :], 0.0).then_inc(own_tap_written, 1)
            for t in range(TAPS):
                pool.wait_ge(own_tap_written, t + 1)
                nc.gpsimd.memset(own_tap[t * G:(t + 1) * G, t:t + 1], 1.0).then_inc(own_tap_written, 1)
            pool.wait_ge(own_tap_written, TAPS + 1)
            pool.wait_ge(ident_zeroed, 1)
            nc.gpsimd.affine_select(out=ident[:, :], in_=ident[:, :], compare_op=ALU.not_equal, fill=1.0, base=0,
                                    pattern=[[-1, P]], channel_multiplier=1).then_inc(ident_ready, 1)
            with pool.Fori(0, B - 1) as b:
                for u in range(UNITS):
                    pool_unit(pool, b, u, False)
            for u in range(UNITS - 1):
                pool_unit(pool, B - 1, u, True)


def kernel(x, L0_conv_w1, L0_conv_gamma, L0_conv_beta, L0_conv_running_mean, L0_conv_running_var, L0_conv_w2,
           L0_conv_b2, L0_conv_bias, L1_conv_beta, L1_conv_gamma):
    import concourse.bacc as bacc
    from concourse.bass_utils import run_bass_kernel_spmd

    w1t, w2, gammat = np.asarray(L0_conv_w1).T, np.asarray(L0_conv_w2), np.asarray(L1_conv_gamma).T
    C, R = w1t.shape
    CD, G, taps = C // SLOTS, 128 // TAPS, w2.reshape(C, -1, R)

    def by_slots(a):
        return np.stack([np.concatenate([a, a[s * CD:(s + 1) * CD]]) for s in range(SLOTS)], 1)

    w2_rows = np.zeros((TAPS, G, C), np.float32)
    w2_rows[:, :R] = taps[:, :TAPS].transpose(1, 2, 0)
    w2_rows[:, R] = np.asarray(L0_conv_b2).reshape(C, -1)[:, :TAPS].T
    bn = np.zeros((TAPS, G, 4), np.float32)
    for i, a in enumerate((L0_conv_gamma, L0_conv_beta, L0_conv_running_mean, L0_conv_running_var)):
        bn[:, :R, i] = np.asarray(a)
    bn[:, R, 1] = 1.0
    bias = by_slots(np.asarray(L0_conv_bias).reshape(-1, 1))
    fields = {
        "w1": by_slots(w1t).reshape(128, -1),
        "w2": by_slots(w2_rows.reshape(128, C).T).transpose(2, 1, 0).reshape(128, -1),
        "bias": bias.reshape(128, SLOTS),
        "bn": bn.reshape(128, 4),
        "beta": np.pad(np.asarray(L1_conv_beta).reshape(-1, 1), ((0, CD), (0, 0))),
        "gamma": np.pad(gammat, ((0, CD), (0, 0))),
    }
    arrays = {
        "x": np.ascontiguousarray(x),
        "par": np.ascontiguousarray(np.concatenate(list(fields.values()), 1)),
        "biasrow": np.ascontiguousarray(bias.reshape(128, SLOTS).T.reshape(1, -1)),
    }
    nc = bacc.Bacc("TRN2", target_bir_lowering=False, num_devices=1)
    aps = {n: nc.dram_tensor(f"in_{n}", a.shape, F32, kind="ExternalInput").ap() for n, a in arrays.items()}
    out = nc.dram_tensor("out_y", arrays["x"].shape, F32, kind="ExternalOutput").ap()
    conv_gdn(nc, out=out, widths=[(name, a.shape[1]) for name, a in fields.items()], **aps)
    r = run_bass_kernel_spmd(nc, [{f"in_{n}": a for n, a in arrays.items()}], core_ids=[0])
    return r.results[0]["out_y"]
```
